# Optimizing a Trainium2 kernel written in Bass

```python
import numpy as np
import jax
import jax.numpy as jnp

def _softmax(x, axis=-1):
    return jax.nn.softmax(x, axis=axis)

def _gelu(x):
    return jax.nn.gelu(x, approximate=True)

def _silu(x):
    return jax.nn.silu(x)

def _sigmoid(x):
    return jax.nn.sigmoid(x)

def _layernorm(x, axis=-1, eps=1e-05):
    m = jnp.mean(x, axis=axis, keepdims=True)
    v = jnp.var(x, axis=axis, keepdims=True)
    return (x - m) / jnp.sqrt(v + eps)

def _scatter_add(tgt, idx, src, axis=0):
    return tgt.at[idx].add(src)

def _segment_sum(src, seg, n):
    return jax.ops.segment_sum(src, seg, n)
kernel_name = 'mk_cond_resid_d2_seqx_r8_f5f0dd'

def setup_inputs(seed: int=0):
    np.random.seed(seed)
    _w = jnp.asarray

    def _rec_inputs():
        import jax
        import jax.numpy as jnp
        _rk = jax.random.key(seed)
        x = -7.109e-05 + 0.9999 * jax.random.normal(jax.random.fold_in(_rk, 1), (64, 32, 512), jnp.float32)
        _lenS = 32 - jax.random.randint(jax.random.fold_in(_rk, 7), (64,), 0, max(1, 32 // 4) + 1, jnp.int32)
        _lenS2 = 32 - jax.random.randint(jax.random.fold_in(_rk, 8), (64,), 0, max(1, 32 // 4) + 1, jnp.int32)
        itok_B_0_15 = jax.random.randint(jax.random.fold_in(_rk, 11), (64,), 0, 16, jnp.int32)
        itok_B_0_2 = jax.random.randint(jax.random.fold_in(_rk, 12), (64,), 0, 3, jnp.int32)
        return (x, itok_B_0_15, itok_B_0_2)
    x, itok_B_0_15, itok_B_0_2 = _rec_inputs()

    def _L0_cond_setup():
        import jax, jax.numpy as jnp
        import numpy as np
        NUM_CONDITIONS = 16
        IN_CH = 32
        OUT_CH = 32
        B = 64
        T = 512
        key = jax.random.key(seed)
        k_x, k_w, k_c = jax.random.split(key, 3)
        x = jax.random.normal(k_x, (B, IN_CH, T), dtype=jnp.float32)
        bound = float(np.sqrt(6.0 / IN_CH))
        weights = jax.random.uniform(k_w, (NUM_CONDITIONS, IN_CH, OUT_CH), dtype=jnp.float32, minval=-bound, maxval=bound)
        condition = jax.random.randint(k_c, (B,), 0, NUM_CONDITIONS, dtype=jnp.int64)
        return {'x': x, 'weights': weights, 'condition': condition}
    _L0_cond_all = _L0_cond_setup()
    _L0_cond_in = {k: v for k, v in _L0_cond_all.items() if k in ('weights',)}
    del _L0_cond_all

    def _L1_cond_setup():
        import jax, jax.numpy as jnp
        import numpy as np
        B, S, D_IN, D_OUT = (4, 256, 512, 512)
        R, NUM_LABELERS = (32, 5)
        LORA_SCALING = 16 / 32
        key = jax.random.key(seed)
        k1, k2, k3, k4, k5 = jax.random.split(key, 5)
        x = jax.random.normal(k1, (B, S, D_IN), dtype=jnp.float32)
        labeler_index = jax.random.randint(k2, (B,), 0, NUM_LABELERS, dtype=jnp.int64)
        W = jax.random.normal(k3, (D_OUT, D_IN), dtype=jnp.float32) * 0.02
        lora_A = jax.random.normal(k4, (NUM_LABELERS, D_IN, R), dtype=jnp.float32) * 0.02
        lora_B_w = jax.random.normal(k5, (D_OUT, R), dtype=jnp.float32) * 0.02
        return {'x': x, 'labeler_index': labeler_index, 'W': W, 'lora_A': lora_A, 'lora_B_w': lora_B_w}
    _L1_cond_all = _L1_cond_setup()
    _L1_cond_in = {k: v for k, v in _L1_cond_all.items() if k in ('W', 'lora_A', 'lora_B_w')}
    del _L1_cond_all
    return {'x': x, 'itok_B_0_15': itok_B_0_15, 'itok_B_0_2': itok_B_0_2, 'L0_cond_weights': _L0_cond_in['weights'], 'L1_cond_W': _L1_cond_in['W'], 'L1_cond_lora_A': _L1_cond_in['lora_A'], 'L1_cond_lora_B_w': _L1_cond_in['lora_B_w']}

def reference(x, itok_B_0_15, itok_B_0_2, L0_cond_weights, L1_cond_W, L1_cond_lora_A, L1_cond_lora_B_w):
    import jax
    import jax.numpy as jnp

    def _L0_cond_ref(x, weights, condition):
        import jax, jax.numpy as jnp
        import numpy as np
        NUM_CONDITIONS = 16
        IN_CH = 32
        OUT_CH = 32
        B = 64
        T = 512
        W = weights[condition]
        return jnp.einsum('bct,bcd->bdt', x, W)

    def _L1_cond_ref(x, labeler_index, W, lora_A, lora_B_w):
        import jax, jax.numpy as jnp
        import numpy as np
        B, S, D_IN, D_OUT = (4, 256, 512, 512)
        R, NUM_LABELERS = (32, 5)
        LORA_SCALING = 16 / 32
        base = jnp.einsum('bsi,oi->bso', x, W)
        labelers_A = lora_A[labeler_index]
        low = jnp.einsum('bsi,bir->bsr', x, labelers_A)
        delta = jnp.einsum('bsr,or->bso', low, lora_B_w) * LORA_SCALING
        return base + delta
    x = x + _L0_cond_ref(x, L0_cond_weights, itok_B_0_15)
    x = x + _L1_cond_ref(x, itok_B_0_2, L1_cond_W, L1_cond_lora_A, L1_cond_lora_B_w)
    return x

_drawn_inputs = setup_inputs


def setup_inputs(seed=0):
    import zlib

    import numpy as np

    out = dict(_drawn_inputs(seed))
    spreads = {}
    factors = {}
    for name, (base, spread) in spreads.items():
        noise = np.random.default_rng([zlib.crc32(name.encode()), seed]).standard_normal(out[name].shape)
        drawn = base * np.exp(spread * noise) if base else spread * noise
        out[name] = jnp.asarray(drawn.astype(out[name].dtype))
    for name, factor in factors.items():
        out[name] = (out[name] * factor).astype(out[name].dtype)
    return out
```

```python
from contextlib import ExitStack

import concourse.bass as bass
from concourse import mybir

F32 = mybir.dt.float32
F32R = mybir.dt.float32r
I32 = mybir.dt.int32
ALU = mybir.AluOpType
COPY = mybir.ActivationFunctionType.Copy

P = 128


def conditioned_lora_kernel(nc, x, cond, label, W0, W, A, Bw, out):
    B, S, T = x.shape
    NL, _, R = A.shape
    O = W.shape[0]
    BT = P // S
    TILES = B // BT
    PAIRS = TILES // 2
    C = T // P
    OC = O // P
    Q = P // R
    ROWS = 2 * P
    LOOPS = PAIRS // 2 - 1
    assert S == R == 32 and NL == Q + 1 and T == O == 512

    x_pair = x.rearrange("(k u b) s t -> k (b s) u t", u=2, b=BT)
    out_pair = out.rearrange("(k u b) s t -> k (b s) u t", u=2, b=BT)
    out_tile = out.rearrange("(k b) s t -> k (b s) t", b=BT)
    W0_rows = W0.rearrange("n c d -> (n c) d")

    with ExitStack() as ctx:
        def sb(name, shape, dt=F32):
            return ctx.enter_context(nc.sbuf_tensor(name, shape, dt))

        def ps(name, shape):
            return ctx.enter_context(nc.psum_tensor(name, shape, F32))

        def sem(name):
            return ctx.enter_context(nc.semaphore(name))

        ident = sb("ident", [P, P])
        fold_id = sb("fold_id", [P, R])
        fold_r = sb("fold_r", [P, Q, R], F32R)
        block = sb("block", [P, BT])
        p_num = sb("p_num", [P, 1])
        group = sb("group", [P, 1])
        row_of = sb("row_of", [P, 1])
        cond_b = sb("cond_b", [P, B], I32)
        label_b = sb("label_b", [P, B], I32)
        w0_row = sb("w0_row", [P, TILES], I32)
        keep = sb("keep", [P, B])
        w_sb = sb("w_sb", [P, OC, T])
        a_sb = sb("a_sb", [P, NL, C, R])
        bw_sb = sb("bw_sb", [P, OC, R])
        bw_rep = sb("bw_rep", [P, OC, Q, R])
        a0_rep = sb("a0_rep", [P, C, Q, R])
        a_diff = sb("a_diff", [P, C, Q, R])
        ad_hi = sb("ad_hi", [P, C, Q, R], F32R)
        ad_lo = sb("ad_lo", [P, C, Q, R], F32R)
        b_stack = sb("b_stack", [P, O], F32R)
        a0_stack = sb("a0_stack", [P, T], F32R)
        m_hi = sb("m_hi", [P, C, O], F32R)
        m_lo = sb("m_lo", [P, C, O], F32R)
        w0_sel = sb("w0_sel", [P, TILES, S])
        x_sb = sb("x_sb", [P, 2, 2, T])
        x_hi = sb("x_hi", [P, 2, 2, T], F32R)
        x_lo = sb("x_lo", [P, 2, 2, T], F32R)
        mix = sb("mix", [P, 2, S])
        mixh = sb("mixh", [P, 2, S], F32R)
        mixl = sb("mixl", [P, 2, S])
        bd_hi = sb("bd_hi", [P, 2, 2, BT, S], F32R)
        bd_lo = sb("bd_lo", [P, 2, 2, BT, S], F32R)
        x1_hi = sb("x1_hi", [P, 2, C, ROWS], F32R)
        x1_lo = sb("x1_lo", [P, 2, C, ROWS], F32R)
        kept = sb("kept", [P, ROWS])
        kept_hi = sb("kept_hi", [P, ROWS], F32R)
        kept_lo = sb("kept_lo", [P, ROWS], F32R)
        low_stack = sb("low_stack", [P, ROWS], F32R)
        y_sb = sb("y_sb", [P, TILES, O])

        p_mix = [ps(f"p_mix{i}", [P, C, P]) for i in range(2)]
        p_y = [ps(f"p_y{i}", [P, O]) for i in range(4)]
        p_low = ps("p_low", [P, O])
        p_fold = ps("p_fold", [P, O])

        s_index_in = sem("s_index_in")
        s_bw_in = sem("s_bw_in")
        s_a_in = sem("s_a_in")
        s_w_in = [sem(f"s_w_in{i}") for i in range(OC)]
        s_x_in = [sem(f"s_x_in{i}") for i in range(2)]
        s_w0_in = [sem(f"s_w0_in{i}") for i in range(3)]
        s_y_out = sem("s_y_out")
        s_pool = sem("s_pool")
        s_dve = sem("s_dve")
        s_group = sem("s_group")
        s_w0_row = sem("s_w0_row")
        s_rep = sem("s_rep")
        s_diag = sem("s_diag")
        s_adiff = sem("s_adiff")
        s_adhi = sem("s_adhi")
        s_adlo = sem("s_adlo")
        s_bT = sem("s_bT")
        s_aT = sem("s_aT")
        s_bhi = sem("s_bhi")
        s_ahi = sem("s_ahi")
        s_stacks = sem("s_stacks")
        s_m = sem("s_m")
        s_mlo = sem("s_mlo")
        s_xhi = sem("s_xhi")
        s_xlo = sem("s_xlo")
        s_bd = sem("s_bd")
        s_mixed = sem("s_mixed")
        s_x1hi = sem("s_x1hi")
        s_x1lo = sem("s_x1lo")
        s_low = sem("s_low")
        s_low_read = sem("s_low_read")
        s_kepthi = sem("s_kepthi")
        s_keptlo = sem("s_keptlo")
        s_fold = sem("s_fold")
        s_foldhi = sem("s_foldhi")
        s_stack = sem("s_stack")
        s_y = sem("s_y")
        s_y_copied = sem("s_y_copied")
        s_last = sem("s_last")

        blk = ctx.enter_context(nc.Block())

        @blk.sync
        def _(sp):
            sp.dma_start(cond_b[:], cond.partition_broadcast(P)).then_inc(s_index_in, 16)
            sp.dma_start(label_b[:], label.partition_broadcast(P)).then_inc(s_index_in, 16)
            sp.dma_start(x_sb[:, 0], x_pair[0]).then_inc(s_x_in[0], 16)
            sp.dma_start(a_sb[:], A.rearrange("l (c p) r -> p l c r", p=P)).then_inc(s_a_in, 16)
            sp.dma_start(x_sb[:, 1], x_pair[1]).then_inc(s_x_in[1], 16)

            def load(p, slot):
                sp.wait_ge(s_xlo, 2 * p - 2)
                sp.dma_start(x_sb[:, slot], x_pair[p]).then_inc(s_x_in[slot], 16)

            def store(p):
                sp.wait_ge(s_y_copied, C + 2 * p + 2)
                sp.dma_start(out_pair[p], y_sb[:, bass.ds(2 * p, 2)]).then_inc(s_y_out, 16)

            with sp.Fori(0, LOOPS) as g:
                for slot in range(2):
                    load(2 * g + slot + 2, slot)
                    store(2 * g + slot)
            store(PAIRS - 2)
            sp.wait_ge(s_y_copied, C + TILES - 1)
            sp.dma_start(out_tile[TILES - 2], y_sb[:, TILES - 2]).then_inc(s_y_out, 16)
            sp.wait_ge(s_last, 1)
            sp.dma_start(out_tile[TILES - 1], y_sb[:, TILES - 1]).then_inc(s_y_out, 16)
            sp.wait_ge(s_y_out, 16 * (PAIRS + 1))

        @blk.gpsimd
        def _(pool):
            nc.gpsimd.iota(p_num[:], pattern=[[0, 1]], base=0, channel_multiplier=1,
                           allow_small_or_imprecise_dtypes=True).then_inc(s_pool, 1)
            pool.wait_ge(s_pool, 1)
            nc.gpsimd.memset(ident[:], 0.0).then_inc(s_pool, 1)
            pool.wait_ge(s_pool, 2)
            nc.gpsimd.affine_select(out=ident[:], in_=ident[:], compare_op=ALU.not_equal, fill=1.0, base=0,
                                    pattern=[[-1, P]], channel_multiplier=1).then_inc(s_pool, 1)
            pool.wait_ge(s_pool, 3)
            nc.gpsimd.memset(fold_id[:], 0.0).then_inc(s_pool, 1)
            for j in range(Q):
                pool.wait_ge(s_pool, 4 + j)
                nc.gpsimd.affine_select(out=fold_id[:], in_=fold_id[:], compare_op=ALU.not_equal, fill=1.0,
                                        base=-R * j, pattern=[[-1, R]], channel_multiplier=1).then_inc(s_pool, 1)
            pool.wait_ge(s_w0_row, BT)
            for t in range(TILES):
                nc.gpsimd.indirect_dma_start(
                    out=w0_sel[:, t, :], out_offset=None, in_=W0_rows,
                    in_offset=bass.IndirectOffsetOnAxis(ap=w0_row[:, t:t + 1], axis=0),
                ).then_inc(s_w0_in[min(t // 2, 2)], 16)

        @blk.scalar
        def _(act):
            act.dma_start(bw_sb[:], Bw.rearrange("(o p) r -> p o r", p=P)).then_inc(s_bw_in, 16)
            for o in range(OC):
                act.dma_start(w_sb[:, o], W[P * o:P * (o + 1), :]).then_inc(s_w_in[o], 16)

            def split_x(p, slot, u):
                nc.scalar.activation(x_hi[:, slot, u], x_sb[:, slot, u], COPY).then_inc(s_xhi, 1)

            def split_x1(t, slot, u):
                act.wait_ge(s_mixed, t + 1)
                nc.scalar.activation(x1_hi[:, slot, :, P * u:P * (u + 1)], p_mix[u][:], COPY).then_inc(s_x1hi, 1)

            act.wait_ge(s_bT, 1)
            nc.scalar.activation(b_stack[:], p_low[:], COPY).then_inc(s_bhi, 1)
            act.wait_ge(s_x_in[0], 16)
            split_x(0, 0, 0)
            act.wait_ge(s_aT, 1)
            nc.scalar.activation(a0_stack[:], p_fold[:], COPY).then_inc(s_ahi, 1)
            split_x(0, 0, 1)
            act.wait_ge(s_adiff, 1)
            nc.scalar.activation(ad_hi[:], a_diff[:], COPY).then_inc(s_adhi, 1)
            for u in range(2):
                split_x1(u, 0, u)
            for c in range(C):
                act.wait_ge(s_m, c + 1)
                nc.scalar.activation(m_hi[:, c], p_y[c][:], COPY).then_inc(s_y_copied, 1)
            act.wait_ge(s_x_in[1], 16)
            for u in range(2):
                split_x(1, 1, u)

            def pair(p, slot, mixes, turn=None):
                splits = turn is not None
                act.wait_ge(s_low_read, p + 2)
                nc.scalar.activation(kept_hi[:], kept[:], COPY).then_inc(s_kepthi, 1)
                for u in range(2):
                    if mixes:
                        split_x1(2 * p + 2 + u, 1 - slot, u)
                    if u == 0:
                        if splits:
                            act.wait_ge(s_x_in[slot], 16 * (turn + 2))
                            split_x(p + 2, slot, 0)
                        act.wait_ge(s_fold, p + 1)
                        nc.scalar.activation(low_stack[:], p_fold[:, 0:ROWS], COPY).then_inc(s_foldhi, 1)
                    elif splits:
                        split_x(p + 2, slot, 1)
                for u in range(2 if mixes else 1):
                    act.wait_ge(s_y, 2 * p + u + 1)
                    nc.scalar.activation(y_sb[:, bass.ds(2 * p + u, 1)],
                                         p_y[2 * slot + u][:].unsqueeze(1), COPY).then_inc(s_y_copied, 1)

            with act.Fori(0, LOOPS) as g:
                for slot in range(2):
                    pair(2 * g + slot, slot, True, turn=g)
            pair(PAIRS - 2, 0, True)
            pair(PAIRS - 1, 1, False)

        @blk.vector
        def _(dve):
            chain = [0]

            def then_wait(ins):
                chain[0] += 1
                ins.then_inc(s_dve, 1)
                dve.wait_ge(s_dve, chain[0])

            def split_x(t, slot, u):
                dve.wait_ge(s_xhi, t + 1)
                nc.vector.tensor_tensor(x_lo[:, slot, u], x_sb[:, slot, u], x_hi[:, slot, u].bitcast(F32),
                                        ALU.subtract).then_inc(s_xlo, 1)

            def split_x1(t, slot, u):
                dve.wait_ge(s_x1hi, t + 1)
                cols = slice(P * u, P * (u + 1))
                nc.vector.tensor_tensor(x1_lo[:, slot, :, cols], p_mix[u][:], x1_hi[:, slot, :, cols].bitcast(F32),
                                        ALU.subtract).then_inc(s_x1lo, 1)

            def block_diagonal(w0, slot, link):
                link(nc.vector.tensor_tensor(mix[:], w0, fold_id[:].unsqueeze(1).broadcast_to([P, 2, S]), ALU.add))
                link(nc.vector.tensor_copy(mixh[:], mix[:]))
                link(nc.vector.tensor_tensor(mixl[:], mix[:], mixh[:].bitcast(F32), ALU.subtract))
                on = block[:].unsqueeze(1).unsqueeze(3).broadcast_to([P, 2, BT, S])
                nc.vector.tensor_tensor(bd_hi[:, slot], mixh[:].bitcast(F32).unsqueeze(2).broadcast_to([P, 2, BT, S]),
                                        on, ALU.mult)
                nc.vector.tensor_tensor(bd_lo[:, slot], mixl[:].unsqueeze(2).broadcast_to([P, 2, BT, S]),
                                        on, ALU.mult).then_inc(s_bd, 1)

            for j in range(BT):
                nc.vector.memset(group[R * j:R * (j + 1)], float(j)).then_inc(s_group, 1)
            nc.vector.memset(block[:], 0.0).then_inc(s_group, 1)
            dve.wait_ge(s_group, BT + 1)
            for j in range(BT):
                nc.vector.memset(block[R * j:R * (j + 1), j:j + 1], 1.0).then_inc(s_group, 1)
            dve.wait_ge(s_pool, 1)
            then_wait(nc.vector.scalar_tensor_tensor(row_of[:], group[:], -float(R), p_num[:], ALU.mult, ALU.add))
            dve.wait_ge(s_index_in, 32)
            cond_v = cond_b[:].rearrange("p (k b) -> p b k", b=BT)
            for j in range(BT):
                quad = slice(R * j, R * (j + 1))
                nc.vector.tensor_scalar(w0_row[quad], cond_v[quad, j], float(S), row_of[quad, 0:1],
                                        ALU.mult, ALU.add).then_inc(s_w0_row, 1)
            nc.vector.tensor_scalar(keep[:], label_b[:], -1.0, group[:, 0:1], ALU.add,
                                    ALU.is_equal).then_inc(s_group, 1)
            dve.wait_ge(s_bw_in, 16)
            nc.vector.tensor_scalar(bw_rep[:], bw_sb[:].unsqueeze(2).broadcast_to([P, OC, Q, R]), 0.5, None,
                                    ALU.mult).then_inc(s_rep, 1)
            dve.wait_ge(s_a_in, 16)
            nc.vector.tensor_copy(a0_rep[:], a_sb[:, 0].unsqueeze(2).broadcast_to([P, C, Q, R])).then_inc(s_rep, 1)
            nc.vector.tensor_tensor(a_diff[:], a_sb[:, 1:NL].rearrange("p l c r -> p c l r"),
                                    a_sb[:, 0].unsqueeze(2).broadcast_to([P, C, Q, R]),
                                    ALU.subtract).then_inc(s_adiff, 1)
            dve.wait_ge(s_bhi, 1)
            for j, done in ((1, s_stacks), (3, s_low_read)):
                quad = slice(R * j, R * (j + 1))
                nc.vector.tensor_tensor(b_stack[quad], p_low[quad], b_stack[quad].bitcast(F32),
                                        ALU.subtract).then_inc(done, 1)
            dve.wait_ge(s_pool, 4 + Q)
            nc.vector.tensor_copy(fold_r[:], fold_id[:].unsqueeze(1).broadcast_to([P, Q, R])).then_inc(s_group, 1)
            dve.wait_ge(s_group, 2 * BT + 3)
            dve.wait_ge(s_ahi, 1)
            nc.vector.tensor_tensor(a0_stack[P // 2:P], p_fold[P // 2:P], a0_stack[P // 2:P].bitcast(F32),
                                    ALU.subtract).then_inc(s_stacks, 1)
            for u in range(2):
                split_x(u, 0, u)
            for o in range(OC):
                dve.wait_ge(s_w_in[o], 16)
                diag = w_sb[:, o, P * o:P * (o + 1)]
                nc.vector.tensor_tensor(diag, diag, ident[:], ALU.add).then_inc(s_diag, 1)
            dve.wait_ge(s_w0_in[0], 32)
            block_diagonal(w0_sel[:, 0:2], 0, then_wait)
            dve.wait_ge(s_adhi, 1)
            nc.vector.tensor_tensor(ad_lo[:], a_diff[:], ad_hi[:].bitcast(F32), ALU.subtract).then_inc(s_adlo, 1)
            for u in range(2):
                split_x1(u, 0, u)
            for c in range(C):
                dve.wait_ge(s_y_copied, c + 1)
                nc.vector.tensor_tensor(m_lo[:, c], p_y[c][:], m_hi[:, c].bitcast(F32),
                                        ALU.subtract).then_inc(s_mlo, 1)
            dve.wait_ge(s_w0_in[1], 32)
            block_diagonal(w0_sel[:, 2:4], 1, then_wait)
            for u in range(2):
                split_x(2 + u, 1, u)
            before_loop = chain[0]

            def pair(p, slot, mixes, splits):
                dve.wait_ge(s_low, p + 1)
                labels = keep[:, bass.ds(2 * BT * p, 2 * BT)].unsqueeze(2).broadcast_to([P, 2 * BT, S])
                nc.vector.tensor_tensor(kept[:].rearrange("p (b s) -> p b s", s=S),
                                        p_low[:, 0:ROWS].rearrange("p (b s) -> p b s", s=S),
                                        labels, ALU.mult).then_inc(s_low_read, 1)
                dve.wait_ge(s_kepthi, p + 1)
                nc.vector.tensor_tensor(kept_lo[:], kept[:], kept_hi[:].bitcast(F32),
                                        ALU.subtract).then_inc(s_keptlo, 1)
                if mixes:
                    split_x1(2 * p + 2, 1 - slot, 0)
                if splits:
                    split_x(2 * p + 4, slot, 0)
                dve.wait_ge(s_foldhi, p + 1)
                nc.vector.tensor_tensor(low_stack[P // 2:P], p_fold[P // 2:P, 0:ROWS],
                                        low_stack[P // 2:P].bitcast(F32), ALU.subtract).then_inc(s_stack, 1)
                if mixes:
                    split_x1(2 * p + 3, 1 - slot, 1)
                if splits:
                    split_x(2 * p + 5, slot, 1)
                    dve.wait_ge(s_w0_in[2], 16 * (TILES - 4))
                    step = [0]

                    def link(ins):
                        step[0] += 1
                        ins.then_inc(s_dve, 1)
                        dve.wait_ge(s_dve, before_loop + 3 * p + step[0])

                    block_diagonal(w0_sel[:, bass.ds(2 * p + 4, 2)], slot, link)

            with dve.Fori(0, LOOPS) as g:
                for slot in range(2):
                    pair(2 * g + slot, slot, True, True)
            pair(PAIRS - 2, 0, True, False)
            pair(PAIRS - 1, 1, False, False)
            dve.wait_ge(s_y, TILES)
            nc.vector.tensor_copy(y_sb[:, TILES - 1], p_y[3][:]).then_inc(s_last, 1)

        @blk.tensor
        def _(pe):
            mm = nc.tensor.matmul

            def mix_tile(t, slot, u):
                pe.wait_ge(s_xlo, t + 1)
                for c in range(C):
                    cols = slice(P * c, P * (c + 1))
                    mm(p_mix[u][:, c], x_hi[:, slot, u, cols], bd_hi[:, slot, u], start=(c == 0), stop=False)
                    mm(p_mix[u][:, c], x_hi[:, slot, u, cols], bd_lo[:, slot, u], start=False, stop=False)
                    last = mm(p_mix[u][:, c], x_lo[:, slot, u, cols], bd_hi[:, slot, u], start=False,
                              stop=(c == C - 1))
                last.then_inc(s_mixed, 1)

            def low_pair(slot):
                for c in range(C):
                    mm(p_low[:, 0:ROWS], ad_hi[:, c], x1_hi[:, slot, c], start=(c == 0), stop=False)
                    mm(p_low[:, 0:ROWS], ad_hi[:, c], x1_lo[:, slot, c], start=False, stop=False)
                    last = mm(p_low[:, 0:ROWS], ad_lo[:, c], x1_hi[:, slot, c], start=False, stop=(c == C - 1))
                last.then_inc(s_low, 1)

            def main_tile(slot, u):
                y = p_y[2 * slot + u]
                rows = slice(P * u, P * (u + 1))
                for c in range(C):
                    mm(y[:], x1_hi[:, slot, c, rows], m_hi[:, c], start=(c == 0), stop=False)
                    mm(y[:], x1_hi[:, slot, c, rows], m_lo[:, c], start=False, stop=False)
                    mm(y[:], x1_lo[:, slot, c, rows], m_hi[:, c], start=False, stop=False)

            def fold_pair():
                mm(p_fold[:, 0:ROWS], fold_r[:], kept_hi[:], start=True, stop=False)
                mm(p_fold[:, 0:ROWS], fold_r[:], kept_lo[:], start=False, stop=True).then_inc(s_fold, 1)

            def delta_tile(slot, u):
                mm(p_y[2 * slot + u][:], low_stack[:, P * u:P * (u + 1)], b_stack[:],
                   start=False, stop=True).then_inc(s_y, 1)

            pe.wait_ge(s_pool, 3)
            pe.wait_ge(s_rep, 1)
            for o in range(OC):
                last = mm(p_low[:, P * o:P * (o + 1)], bw_rep[:, o], ident[:], start=(o == 0), stop=(o == OC - 1))
            last.then_inc(s_bT, 1)
            pe.wait_ge(s_rep, 2)
            for c in range(C):
                last = mm(p_fold[:, P * c:P * (c + 1)], a0_rep[:, c], ident[:], start=(c == 0), stop=(c == C - 1))
            last.then_inc(s_aT, 1)
            pe.wait_ge(s_stacks, 2)
            pe.wait_ge(s_low_read, 1)
            for c in range(C):
                mm(p_y[c][:], a0_stack[:, P * c:P * (c + 1)], b_stack[:], start=True, stop=False)
            for o in range(OC):
                pe.wait_ge(s_diag, o + 1)
                for c in range(C):
                    last = mm(p_y[c][:, P * o:P * (o + 1)], w_sb[:, o, P * c:P * (c + 1)], ident[:],
                              start=False, stop=(o == OC - 1))
                    if o == OC - 1:
                        last.then_inc(s_m, 1)
            pe.wait_ge(s_bd, 1)
            mix_tile(0, 0, 0)
            mix_tile(1, 0, 1)
            pe.wait_ge(s_adlo, 1)
            pe.wait_ge(s_mlo, C)

            def pair(p, slot, mixes, before):
                pe.wait_ge(s_x1lo, 2 * p + 2)
                pe.wait_ge(s_low_read, p + 1)
                low_pair(slot)
                if mixes:
                    pe.wait_ge(s_bd, p + 2)
                    mix_tile(2 * p + 2, 1 - slot, 0)
                pe.wait_ge(s_y_copied, C + 2 * before)
                main_tile(slot, 0)
                pe.wait_ge(s_keptlo, p + 1)
                fold_pair()
                if mixes:
                    mix_tile(2 * p + 3, 1 - slot, 1)
                main_tile(slot, 1)
                pe.wait_ge(s_stack, p + 1)
                delta_tile(slot, 0)
                delta_tile(slot, 1)

            with pe.Fori(0, LOOPS) as g:
                for slot in range(2):
                    pair(2 * g + slot, slot, True, 2 * g)
            pair(PAIRS - 2, 0, True, PAIRS - 2)
            pair(PAIRS - 1, 1, False, PAIRS - 2)


_INS = ["x", "itok_B_0_15", "itok_B_0_2", "L0_cond_weights", "L1_cond_W", "L1_cond_lora_A", "L1_cond_lora_B_w"]


def kernel(**inputs):
    import numpy as np
    import concourse.bacc as bacc
    from concourse.bass_utils import run_bass_kernel_spmd

    nc = bacc.Bacc("TRN2", target_bir_lowering=False, num_devices=1)
    arrays, args = {}, []
    for name in _INS:
        a = np.ascontiguousarray(inputs[name])
        arrays[f"in_{name}"] = a
        args.append(nc.dram_tensor(f"in_{name}", a.shape, mybir.dt.from_np(a.dtype), kind="ExternalInput").ap())
    shape = inputs["x"].shape
    out = nc.dram_tensor("out_0", shape, F32, kind="ExternalOutput").ap()
    conditioned_lora_kernel(nc, *args, out)
    r = run_bass_kernel_spmd(nc, [arrays], core_ids=[0])
    return r.results[0]["out_0"]
```

```python
from contextlib import ExitStack

import concourse.bass as bass
from concourse import mybir

F32 = mybir.dt.float32
F32R = mybir.dt.float32r
I32 = mybir.dt.int32
ALU = mybir.AluOpType
COPY = mybir.ActivationFunctionType.Copy

P = 128


def conditioned_lora_kernel(nc, x, cond, label, W0, W, A, Bw, out):
    B, S, T = x.shape
    NL, _, R = A.shape
    O = W.shape[0]
    BT = P // S
    TILES = B // BT
    PAIRS = TILES // 2
    C = T // P
    OC = O // P
    Q = P // R
    ROWS = 2 * P
    LOOPS = PAIRS // 2 - 1
    assert S == R == 32 and NL == Q + 1 and T == O == 512

    x_pair = x.rearrange("(k u b) s t -> k (b s) u t", u=2, b=BT)
    out_pair = out.rearrange("(k u b) s t -> k (b s) u t", u=2, b=BT)
    out_tile = out.rearrange("(k b) s t -> k (b s) t", b=BT)
    W0_rows = W0.rearrange("n c d -> (n c) d")

    with ExitStack() as ctx:
        def sb(name, shape, dt=F32):
            return ctx.enter_context(nc.sbuf_tensor(name, shape, dt))

        def ps(name, shape):
            return ctx.enter_context(nc.psum_tensor(name, shape, F32))

        def sem(name):
            return ctx.enter_context(nc.semaphore(name))

        ident = sb("ident", [P, P])
        fold_id = sb("fold_id", [P, R])
        fold_r = sb("fold_r", [P, Q, R], F32R)
        block = sb("block", [P, BT])
        p_num = sb("p_num", [P, 1])
        group = sb("group", [P, 1])
        row_of = sb("row_of", [P, 1])
        cond_b = sb("cond_b", [P, B], I32)
        label_b = sb("label_b", [P, B], I32)
        w0_row = sb("w0_row", [P, TILES], I32)
        keep = sb("keep", [P, B])
        w_sb = sb("w_sb", [P, OC, T])
        a_sb = sb("a_sb", [P, NL, C, R])
        bw_sb = sb("bw_sb", [P, OC, R])
        bw_rep = sb("bw_rep", [P, OC, Q, R])
        a0_rep = sb("a0_rep", [P, C, Q, R])
        a_diff = sb("a_diff", [P, C, Q, R])
        ad_hi = sb("ad_hi", [P, C, Q, R], F32R)
        ad_lo = sb("ad_lo", [P, C, Q, R], F32R)
        b_stack = sb("b_stack", [P, O], F32R)
        a0_stack = sb("a0_stack", [P, T], F32R)
        m_hi = sb("m_hi", [P, C, O], F32R)
        m_lo = sb("m_lo", [P, C, O], F32R)
        w0_sel = sb("w0_sel", [P, TILES, S])
        x_sb = sb("x_sb", [P, 2, 2, T])
        mix = sb("mix", [P, 2, S])
        diag = sb("diag", [P, 2, 2, BT, S])
        x1_hi = sb("x1_hi", [P, 2, C, ROWS], F32R)
        x1_lo = sb("x1_lo", [P, 2, C, ROWS], F32R)
        kept = sb("kept", [P, ROWS])
        kept_hi = sb("kept_hi", [P, ROWS], F32R)
        kept_lo = sb("kept_lo", [P, ROWS], F32R)
        low_stack = sb("low_stack", [P, ROWS], F32R)
        y_sb = sb("y_sb", [P, TILES, O])

        p_mix = [ps(f"p_mix{i}", [P, C, P]) for i in range(2)]
        p_y = [ps(f"p_y{i}", [P, O]) for i in range(4)]
        p_low = ps("p_low", [P, O])
        p_fold = ps("p_fold", [P, O])

        s_cond_in = sem("s_cond_in")
        s_label_in = sem("s_label_in")
        s_bw_in = sem("s_bw_in")
        s_a0_in = sem("s_a0_in")
        s_a_in = sem("s_a_in")
        s_w_in = [sem(f"s_w_in{i}") for i in range(OC)]
        s_x_in = [sem(f"s_x_in{i}") for i in range(2)]
        s_w0_in = [sem(f"s_w0_in{i}") for i in range(3)]
        s_y_out = sem("s_y_out")
        s_pool = sem("s_pool")
        s_dve = sem("s_dve")
        s_group = sem("s_group")
        s_w0_row = sem("s_w0_row")
        s_rep = sem("s_rep")
        s_diag = sem("s_diag")
        s_adiff = sem("s_adiff")
        s_adhi = sem("s_adhi")
        s_adlo = sem("s_adlo")
        s_bT = sem("s_bT")
        s_aT = sem("s_aT")
        s_bhi = sem("s_bhi")
        s_ahi = sem("s_ahi")
        s_stacks = sem("s_stacks")
        s_m = sem("s_m")
        s_mlo = sem("s_mlo")
        s_bd = sem("s_bd")
        s_mixed = sem("s_mixed")
        s_x1hi = sem("s_x1hi")
        s_x1lo = sem("s_x1lo")
        s_low = sem("s_low")
        s_low_read = sem("s_low_read")
        s_kepthi = sem("s_kepthi")
        s_keptlo = sem("s_keptlo")
        s_fold = sem("s_fold")
        s_foldhi = sem("s_foldhi")
        s_stack = sem("s_stack")
        s_y = sem("s_y")
        s_y_copied = sem("s_y_copied")
        s_last = sem("s_last")

        blk = ctx.enter_context(nc.Block())

        @blk.sync
        def _(sp):
            A_v = A.rearrange("l (c p) r -> p l c r", p=P)
            sp.dma_start(cond_b[:], cond.partition_broadcast(P)).then_inc(s_cond_in, 16)
            for o in range(1, OC):
                sp.dma_start(w_sb[:, o], W[P * o:P * (o + 1), :]).then_inc(s_w_in[o], 16)
            sp.dma_start(a_sb[:, 0], A_v[:, 0]).then_inc(s_a0_in, 16)
            sp.dma_start(x_sb[:, 0], x_pair[0]).then_inc(s_x_in[0], 16)
            sp.dma_start(label_b[:], label.partition_broadcast(P)).then_inc(s_label_in, 16)
            sp.dma_start(a_sb[:, 1:NL], A_v[:, 1:NL]).then_inc(s_a_in, 16)
            sp.wait_ge(s_w0_in[0], 32)
            sp.dma_start(x_sb[:, 1], x_pair[1]).then_inc(s_x_in[1], 16)

            def load(p, slot):
                sp.wait_ge(s_mixed, 2 * p - 2)
                sp.dma_start(x_sb[:, slot], x_pair[p]).then_inc(s_x_in[slot], 16)

            def store(p):
                sp.wait_ge(s_y_copied, C + 2 * p + 2)
                sp.dma_start(out_pair[p], y_sb[:, bass.ds(2 * p, 2)]).then_inc(s_y_out, 16)

            with sp.Fori(0, LOOPS) as g:
                for slot in range(2):
                    load(2 * g + slot + 2, slot)
                    store(2 * g + slot)
            store(PAIRS - 2)
            sp.wait_ge(s_y_copied, C + TILES - 1)
            sp.dma_start(out_tile[TILES - 2], y_sb[:, TILES - 2]).then_inc(s_y_out, 16)
            sp.wait_ge(s_last, 1)
            sp.dma_start(out_tile[TILES - 1], y_sb[:, TILES - 1]).then_inc(s_y_out, 16)
            sp.wait_ge(s_y_out, 16 * (PAIRS + 1))

        @blk.gpsimd
        def _(pool):
            nc.gpsimd.iota(p_num[:], pattern=[[0, 1]], base=0, channel_multiplier=1,
                           allow_small_or_imprecise_dtypes=True).then_inc(s_pool, 1)
            pool.wait_ge(s_pool, 1)
            nc.gpsimd.memset(ident[:], 0.0).then_inc(s_pool, 1)
            pool.wait_ge(s_pool, 2)
            nc.gpsimd.affine_select(out=ident[:], in_=ident[:], compare_op=ALU.not_equal, fill=1.0, base=0,
                                    pattern=[[-1, P]], channel_multiplier=1).then_inc(s_pool, 1)
            pool.wait_ge(s_pool, 3)
            nc.gpsimd.memset(fold_id[:], 0.0).then_inc(s_pool, 1)
            for j in range(Q):
                pool.wait_ge(s_pool, 4 + j)
                nc.gpsimd.affine_select(out=fold_id[:], in_=fold_id[:], compare_op=ALU.not_equal, fill=1.0,
                                        base=-R * j, pattern=[[-1, R]], channel_multiplier=1).then_inc(s_pool, 1)
            pool.wait_ge(s_w0_row, BT)
            for t in range(TILES):
                nc.gpsimd.indirect_dma_start(
                    out=w0_sel[:, t, :], out_offset=None, in_=W0_rows,
                    in_offset=bass.IndirectOffsetOnAxis(ap=w0_row[:, t:t + 1], axis=0),
                ).then_inc(s_w0_in[min(t // 2, 2)], 16)

        @blk.scalar
        def _(act):
            act.dma_start(w_sb[:, 0], W[0:P, :]).then_inc(s_w_in[0], 16)
            act.dma_start(bw_sb[:], Bw.rearrange("(o p) r -> p o r", p=P)).then_inc(s_bw_in, 16)

            def split_x1(t, slot, u):
                act.wait_ge(s_mixed, t + 1)
                nc.scalar.activation(x1_hi[:, slot, :, P * u:P * (u + 1)], p_mix[u][:], COPY).then_inc(s_x1hi, 1)

            act.wait_ge(s_bT, 1)
            nc.scalar.activation(b_stack[:], p_low[:], COPY).then_inc(s_bhi, 1)
            act.wait_ge(s_aT, 1)
            nc.scalar.activation(a0_stack[:], p_fold[:], COPY).then_inc(s_ahi, 1)
            for u in range(2):
                split_x1(u, 0, u)
            act.wait_ge(s_adiff, 1)
            nc.scalar.activation(ad_hi[:], a_diff[:], COPY).then_inc(s_adhi, 1)
            for c in range(C):
                act.wait_ge(s_m, c + 1)
                nc.scalar.activation(m_hi[:, c], p_y[c][:], COPY).then_inc(s_y_copied, 1)

            def pair(p, slot, mixes):
                act.wait_ge(s_low_read, p + 2)
                nc.scalar.activation(kept_hi[:], kept[:], COPY).then_inc(s_kepthi, 1)
                for u in range(2):
                    if mixes:
                        split_x1(2 * p + 2 + u, 1 - slot, u)
                    if u == 0:
                        act.wait_ge(s_fold, p + 1)
                        nc.scalar.activation(low_stack[:], p_fold[:, 0:ROWS], COPY).then_inc(s_foldhi, 1)
                for u in range(2 if mixes else 1):
                    act.wait_ge(s_y, 2 * p + u + 1)
                    nc.scalar.activation(y_sb[:, bass.ds(2 * p + u, 1)],
                                         p_y[2 * slot + u][:].unsqueeze(1), COPY).then_inc(s_y_copied, 1)

            with act.Fori(0, LOOPS) as g:
                for slot in range(2):
                    pair(2 * g + slot, slot, True)
            pair(PAIRS - 2, 0, True)
            pair(PAIRS - 1, 1, False)

        @blk.vector
        def _(dve):
            chain = [0]

            def then_wait(ins):
                chain[0] += 1
                ins.then_inc(s_dve, 1)
                dve.wait_ge(s_dve, chain[0])

            def split_x1(t, slot, u):
                dve.wait_ge(s_x1hi, t + 1)
                cols = slice(P * u, P * (u + 1))
                nc.vector.tensor_tensor(x1_lo[:, slot, :, cols], p_mix[u][:], x1_hi[:, slot, :, cols].bitcast(F32),
                                        ALU.subtract).then_inc(s_x1lo, 1)

            def block_diagonal(w0, slot, link):
                link(nc.vector.tensor_tensor(mix[:], w0, fold_id[:].unsqueeze(1).broadcast_to([P, 2, S]), ALU.add))
                nc.vector.tensor_tensor(diag[:, slot], mix[:].unsqueeze(2).broadcast_to([P, 2, BT, S]),
                                        block[:].unsqueeze(1).unsqueeze(3).broadcast_to([P, 2, BT, S]),
                                        ALU.mult).then_inc(s_bd, 1)

            for j in range(BT):
                nc.vector.memset(group[R * j:R * (j + 1)], float(j)).then_inc(s_group, 1)
            nc.vector.memset(block[:], 0.0).then_inc(s_group, 1)
            dve.wait_ge(s_group, BT + 1)
            for j in range(BT):
                nc.vector.memset(block[R * j:R * (j + 1), j:j + 1], 1.0).then_inc(s_group, 1)
            dve.wait_ge(s_pool, 1)
            then_wait(nc.vector.scalar_tensor_tensor(row_of[:], group[:], -float(R), p_num[:], ALU.mult, ALU.add))
            dve.wait_ge(s_cond_in, 16)
            cond_v = cond_b[:].rearrange("p (k b) -> p b k", b=BT)
            for j in range(BT):
                quad = slice(R * j, R * (j + 1))
                nc.vector.tensor_scalar(w0_row[quad], cond_v[quad, j], float(S), row_of[quad, 0:1],
                                        ALU.mult, ALU.add).then_inc(s_w0_row, 1)

            def add_identity(o):
                dve.wait_ge(s_w_in[o], 16)
                w_diag = w_sb[:, o, P * o:P * (o + 1)]
                nc.vector.tensor_tensor(w_diag, w_diag, ident[:], ALU.add).then_inc(s_diag, 1)

            dve.wait_ge(s_pool, 4 + Q)
            add_identity(0)
            dve.wait_ge(s_bw_in, 16)
            nc.vector.tensor_scalar(bw_rep[:], bw_sb[:].unsqueeze(2).broadcast_to([P, OC, Q, R]), 0.5, None,
                                    ALU.mult).then_inc(s_rep, 1)
            add_identity(1)
            nc.vector.tensor_copy(fold_r[:], fold_id[:].unsqueeze(1).broadcast_to([P, Q, R])).then_inc(s_group, 1)
            add_identity(2)
            dve.wait_ge(s_bhi, 1)
            for j, done in ((1, s_stacks), (3, s_low_read)):
                quad = slice(R * j, R * (j + 1))
                nc.vector.tensor_tensor(b_stack[quad], p_low[quad], b_stack[quad].bitcast(F32),
                                        ALU.subtract).then_inc(done, 1)
            add_identity(3)
            dve.wait_ge(s_a0_in, 16)
            nc.vector.tensor_copy(a0_rep[:], a_sb[:, 0].unsqueeze(2).broadcast_to([P, C, Q, R])).then_inc(s_rep, 1)
            dve.wait_ge(s_group, 2 * BT + 2)
            dve.wait_ge(s_w0_in[0], 32)
            block_diagonal(w0_sel[:, 0:2], 0, then_wait)
            dve.wait_ge(s_ahi, 1)
            nc.vector.tensor_tensor(a0_stack[P // 2:P], p_fold[P // 2:P], a0_stack[P // 2:P].bitcast(F32),
                                    ALU.subtract).then_inc(s_stacks, 1)
            dve.wait_ge(s_a_in, 16)
            nc.vector.tensor_tensor(a_diff[:], a_sb[:, 1:NL].rearrange("p l c r -> p c l r"),
                                    a_sb[:, 0].unsqueeze(2).broadcast_to([P, C, Q, R]),
                                    ALU.subtract).then_inc(s_adiff, 1)
            dve.wait_ge(s_label_in, 16)
            nc.vector.tensor_scalar(keep[:], label_b[:], -1.0, group[:, 0:1], ALU.add,
                                    ALU.is_equal).then_inc(s_group, 1)
            for u in range(2):
                split_x1(u, 0, u)
            dve.wait_ge(s_adhi, 1)
            nc.vector.tensor_tensor(ad_lo[:], a_diff[:], ad_hi[:].bitcast(F32), ALU.subtract).then_inc(s_adlo, 1)
            for c in range(C):
                dve.wait_ge(s_y_copied, c + 1)
                nc.vector.tensor_tensor(m_lo[:, c], p_y[c][:], m_hi[:, c].bitcast(F32),
                                        ALU.subtract).then_inc(s_mlo, 1)
            dve.wait_ge(s_group, 2 * BT + 3)
            dve.wait_ge(s_w0_in[1], 32)
            block_diagonal(w0_sel[:, 2:4], 1, then_wait)
            before_loop = chain[0]

            def pair(p, slot, mixes, splits):
                dve.wait_ge(s_low, p + 1)
                labels = keep[:, bass.ds(2 * BT * p, 2 * BT)].unsqueeze(2).broadcast_to([P, 2 * BT, S])
                nc.vector.tensor_tensor(kept[:].rearrange("p (b s) -> p b s", s=S),
                                        p_low[:, 0:ROWS].rearrange("p (b s) -> p b s", s=S),
                                        labels, ALU.mult).then_inc(s_low_read, 1)
                dve.wait_ge(s_kepthi, p + 1)
                nc.vector.tensor_tensor(kept_lo[:], kept[:], kept_hi[:].bitcast(F32),
                                        ALU.subtract).then_inc(s_keptlo, 1)
                if mixes:
                    split_x1(2 * p + 2, 1 - slot, 0)
                dve.wait_ge(s_foldhi, p + 1)
                nc.vector.tensor_tensor(low_stack[P // 2:P], p_fold[P // 2:P, 0:ROWS],
                                        low_stack[P // 2:P].bitcast(F32), ALU.subtract).then_inc(s_stack, 1)
                if mixes:
                    split_x1(2 * p + 3, 1 - slot, 1)
                if splits:
                    dve.wait_ge(s_w0_in[2], 16 * (TILES - 4))
                    step = [0]

                    def link(ins):
                        step[0] += 1
                        ins.then_inc(s_dve, 1)
                        dve.wait_ge(s_dve, before_loop + p + step[0])

                    block_diagonal(w0_sel[:, bass.ds(2 * p + 4, 2)], slot, link)

            with dve.Fori(0, LOOPS) as g:
                for slot in range(2):
                    pair(2 * g + slot, slot, True, True)
            pair(PAIRS - 2, 0, True, False)
            pair(PAIRS - 1, 1, False, False)
            dve.wait_ge(s_y, TILES)
            nc.vector.tensor_copy(y_sb[:, TILES - 1], p_y[3][:]).then_inc(s_last, 1)

        @blk.tensor
        def _(pe):
            mm = nc.tensor.matmul

            def mix_tile(slot, u):
                for c in range(C):
                    last = mm(p_mix[u][:, c], x_sb[:, slot, u, P * c:P * (c + 1)], diag[:, slot, u],
                              start=(c == 0), stop=(c == C - 1))
                last.then_inc(s_mixed, 1)

            def low_pair(slot):
                for c in range(C):
                    mm(p_low[:, 0:ROWS], ad_hi[:, c], x1_hi[:, slot, c], start=(c == 0), stop=False)
                    mm(p_low[:, 0:ROWS], ad_hi[:, c], x1_lo[:, slot, c], start=False, stop=False)
                    last = mm(p_low[:, 0:ROWS], ad_lo[:, c], x1_hi[:, slot, c], start=False, stop=(c == C - 1))
                last.then_inc(s_low, 1)

            def main_tile(slot, u):
                y = p_y[2 * slot + u]
                rows = slice(P * u, P * (u + 1))
                for c in range(C):
                    pe.wait_ge(s_mlo, c + 1 if slot == u == 0 else C)
                    mm(y[:], x1_hi[:, slot, c, rows], m_hi[:, c], start=(c == 0), stop=False)
                    mm(y[:], x1_hi[:, slot, c, rows], m_lo[:, c], start=False, stop=False)
                    mm(y[:], x1_lo[:, slot, c, rows], m_hi[:, c], start=False, stop=False)

            def fold_pair():
                mm(p_fold[:, 0:ROWS], fold_r[:], kept_hi[:], start=True, stop=False)
                mm(p_fold[:, 0:ROWS], fold_r[:], kept_lo[:], start=False, stop=True).then_inc(s_fold, 1)

            def delta_tile(slot, u):
                mm(p_y[2 * slot + u][:], low_stack[:, P * u:P * (u + 1)], b_stack[:],
                   start=False, stop=True).then_inc(s_y, 1)

            def transpose_w(o):
                pe.wait_ge(s_diag, o + 1)
                for c in range(C):
                    mm(p_y[c][:, P * o:P * (o + 1)], w_sb[:, o, P * c:P * (c + 1)], ident[:],
                       start=(o == 0), stop=False)

            pe.wait_ge(s_pool, 3)
            transpose_w(0)
            pe.wait_ge(s_rep, 1)
            for o in range(OC):
                last = mm(p_low[:, P * o:P * (o + 1)], bw_rep[:, o], ident[:], start=(o == 0), stop=(o == OC - 1))
            last.then_inc(s_bT, 1)
            for o in range(1, OC):
                transpose_w(o)
            pe.wait_ge(s_rep, 2)
            for c in range(C):
                last = mm(p_fold[:, P * c:P * (c + 1)], a0_rep[:, c], ident[:], start=(c == 0), stop=(c == C - 1))
            last.then_inc(s_aT, 1)
            pe.wait_ge(s_bd, 1)
            pe.wait_ge(s_x_in[0], 16)
            mix_tile(0, 0)
            mix_tile(0, 1)
            pe.wait_ge(s_stacks, 2)
            pe.wait_ge(s_low_read, 1)
            for c in range(C):
                mm(p_y[c][:], a0_stack[:, P * c:P * (c + 1)], b_stack[:], start=False, stop=True).then_inc(s_m, 1)
            pe.wait_ge(s_adlo, 1)

            def pair(p, slot, before, landed=None):
                mixes = landed is not None
                pe.wait_ge(s_x1lo, 2 * p + 2)
                pe.wait_ge(s_low_read, p + 1)
                low_pair(slot)
                if mixes:
                    pe.wait_ge(s_bd, p + 2)
                    pe.wait_ge(s_x_in[1 - slot], 16 * landed)
                    mix_tile(1 - slot, 0)
                pe.wait_ge(s_y_copied, C + 2 * before)
                main_tile(slot, 0)
                pe.wait_ge(s_keptlo, p + 1)
                fold_pair()
                if mixes:
                    mix_tile(1 - slot, 1)
                main_tile(slot, 1)
                pe.wait_ge(s_stack, p + 1)
                delta_tile(slot, 0)
                delta_tile(slot, 1)

            with pe.Fori(0, LOOPS) as g:
                for slot in range(2):
                    pair(2 * g + slot, slot, 2 * g, g + 1 + slot)
            pair(PAIRS - 2, 0, PAIRS - 2, PAIRS // 2)
            pair(PAIRS - 1, 1, PAIRS - 2)


_INS = ["x", "itok_B_0_15", "itok_B_0_2", "L0_cond_weights", "L1_cond_W", "L1_cond_lora_A", "L1_cond_lora_B_w"]


def kernel(**inputs):
    import numpy as np
    import concourse.bacc as bacc
    from concourse.bass_utils import run_bass_kernel_spmd

    nc = bacc.Bacc("TRN2", target_bir_lowering=False, num_devices=1)
    arrays, args = {}, []
    for name in _INS:
        a = np.ascontiguousarray(inputs[name])
        arrays[f"in_{name}"] = a
        args.append(nc.dram_tensor(f"in_{name}", a.shape, mybir.dt.from_np(a.dtype), kind="ExternalInput").ap())
    shape = inputs["x"].shape
    out = nc.dram_tensor("out_0", shape, F32, kind="ExternalOutput").ap()
    conditioned_lora_kernel(nc, *args, out)
    r = run_bass_kernel_spmd(nc, [arrays], core_ids=[0])
    return r.results[0]["out_0"]
```

```python
from contextlib import ExitStack

import concourse.bass as bass
from concourse import mybir

F32 = mybir.dt.float32
F32R = mybir.dt.float32r
I32 = mybir.dt.int32
ALU = mybir.AluOpType
COPY = mybir.ActivationFunctionType.Copy

P = 128


def conditioned_lora_kernel(nc, x, cond, label, W0, W, A, Bw, out):
    B, S, T = x.shape
    NL, _, R = A.shape
    O = W.shape[0]
    BT = P // S
    TILES = B // BT
    PAIRS = TILES // 2
    C = T // P
    OC = O // P
    Q = P // R
    ROWS = 2 * P
    WARM = 7
    LOOPS = PAIRS // 2 - 1
    assert S == R == 32 and NL == Q + 1 and T == O == 512

    J = T // Q
    assert J == P and C == J // R
    x_pair = x.rearrange("(k b) s (q j) -> k q s b j", b=2 * BT, q=Q)
    A_cols = A.rearrange("l (p c) r -> p l (c r)", c=C)
    out_pair = out.rearrange("(k u b) s t -> k (b s) u t", u=2, b=BT)
    out_tile = out.rearrange("(k b) s t -> k (b s) t", b=BT)
    W0_rows = W0.rearrange("n c d -> (n c) d")

    with ExitStack() as ctx:
        def sb(name, shape, dt=F32):
            return ctx.enter_context(nc.sbuf_tensor(name, shape, dt))

        def ps(name, shape):
            return ctx.enter_context(nc.psum_tensor(name, shape, F32))

        def sem(name):
            return ctx.enter_context(nc.semaphore(name))

        ident = sb("ident", [P, P])
        fold_id = sb("fold_id", [P, R])
        fold_r = sb("fold_r", [P, Q, R], F32R)
        block = sb("block", [P, BT])
        p_num = sb("p_num", [P, 1])
        group = sb("group", [P, 1])
        row_of = sb("row_of", [P, 1])
        cond_b = sb("cond_b", [P, B], I32)
        label_b = sb("label_b", [P, B], I32)
        w0_row = sb("w0_row", [P, TILES], I32)
        keep = sb("keep", [P, B])
        w_sb = sb("w_sb", [P, OC, T])
        a_sb = sb("a_sb", [P, NL, C, R])
        bw_sb = sb("bw_sb", [P, OC, R])
        bw_rep = sb("bw_rep", [P, OC, Q, R])
        a0_rep = sb("a0_rep", [P, C, Q, R])
        a_diff = sb("a_diff", [P, C, Q, R])
        ad_hi = sb("ad_hi", [P, C, Q, R], F32R)
        ad_lo = sb("ad_lo", [P, C, Q, R], F32R)
        b_hi = sb("b_hi", [P, O], F32R)
        a0_hi = sb("a0_hi", [P, T], F32R)
        b_lo_groups = sb("b_lo_groups", [P, 1])
        a_lo_groups = sb("a_lo_groups", [P, 1])
        b_negative = sb("b_negative", [P, P], F32R)
        a_negative = sb("a_negative", [P, P], F32R)
        b_stack = sb("b_stack", [P, O], F32R)
        a0_stack = sb("a0_stack", [P, T], F32R)
        m_hi = sb("m_hi", [P, C, O], F32R)
        m_lo = sb("m_lo", [P, C, O], F32R)
        w0_sel = sb("w0_sel", [P, TILES, S])
        x_sb = sb("x_sb", [P, 2, 2, BT, J])
        xt = sb("xt", [P, 2, C, P])
        xt_hi = sb("xt_hi", [P, 2, C, ROWS], F32R)
        xt_lo = sb("xt_lo", [P, 2, C, ROWS], F32R)
        mix = sb("mix", [P, 2, 2, S])
        diag = sb("diag", [P, 2, 2, BT, S])
        diag_hi = sb("diag_hi", [P, 2, 2, BT, S], F32R)
        diag_lo = sb("diag_lo", [P, 2, 2, BT, S], F32R)
        u_hi = sb("u_hi", [P, 2, O], F32R)
        u_lo = sb("u_lo", [P, 2, O], F32R)
        kept = sb("kept", [P, ROWS])
        kept_hi = sb("kept_hi", [P, ROWS], F32R)
        kept_lo = sb("kept_lo", [P, ROWS], F32R)
        low_stack = sb("low_stack", [P, ROWS], F32R)
        y_sb = sb("y_sb", [P, TILES, O])

        p_u = [ps(f"p_u{i}", [P, O]) for i in range(4)]
        p_y = [ps(f"p_y{i}", [P, O]) for i in range(2)]
        p_low = ps("p_low", [P, O])
        p_fold = ps("p_fold", [P, O])

        s_cond_in = sem("s_cond_in")
        s_label_in = sem("s_label_in")
        s_bw_in = sem("s_bw_in")
        s_a_in = sem("s_a_in")
        s_w_in = [sem(f"s_w_in{i}") for i in range(OC)]
        s_x_in = [sem(f"s_x_in{i}") for i in range(2)]
        s_w0_in = [sem(f"s_w0_in{i}") for i in range(2)]
        s_y_out = sem("s_y_out")
        s_pool = sem("s_pool")
        s_dve = sem("s_dve")
        s_group = sem("s_group")
        s_w0_row = sem("s_w0_row")
        s_rep = sem("s_rep")
        s_diag = sem("s_diag")
        s_adiff = sem("s_adiff")
        s_adhi = sem("s_adhi")
        s_adlo = sem("s_adlo")
        s_bT = sem("s_bT")
        s_aT = sem("s_aT")
        s_stack_hi = sem("s_stack_hi")
        s_negative = sem("s_negative")
        s_less_hi = sem("s_less_hi")
        s_m = sem("s_m")
        s_mlo = sem("s_mlo")
        s_xt = sem("s_xt")
        s_xhi = sem("s_xhi")
        s_xlo = sem("s_xlo")
        s_diag32 = sem("s_diag32")
        s_diaghi = sem("s_diaghi")
        s_diaglo = sem("s_diaglo")
        s_low = sem("s_low")
        s_kept = sem("s_kept")
        s_kepthi = sem("s_kepthi")
        s_keptlo = sem("s_keptlo")
        s_fold = sem("s_fold")
        s_foldhi = sem("s_foldhi")
        s_stack = sem("s_stack")
        s_u = sem("s_u")
        s_uhi = sem("s_uhi")
        s_ulo = sem("s_ulo")
        s_y = sem("s_y")
        s_y_copied = sem("s_y_copied")
        s_last = sem("s_last")

        left, right = slice(0, O // 2), slice(O // 2, O)

        blk = ctx.enter_context(nc.Block())

        @blk.sync
        def _(sp):
            sp.dma_start(bw_sb[:], Bw.rearrange("(o p) r -> p o r", p=P)).then_inc(s_bw_in, 16)
            sp.dma_start(cond_b[:], cond.partition_broadcast(P)).then_inc(s_cond_in, 16)

            def load(p, slot):
                for q in range(Q):
                    sp.dma_start(x_sb[R * q:R * (q + 1), slot].rearrange("s u b j -> s (u b) j"),
                                 x_pair[p, q]).then_inc(s_x_in[slot], 16)

            load(0, 0)
            for o in range(1, OC):
                sp.dma_start(w_sb[:, o], W[P * o:P * (o + 1), :]).then_inc(s_w_in[o], 16)
            sp.dma_start(label_b[:], label.partition_broadcast(P)).then_inc(s_label_in, 16)
            load(1, 1)

            def store(p):
                sp.wait_ge(s_y_copied, 2 + 2 * p + 2)
                sp.dma_start(out_pair[p], y_sb[:, bass.ds(2 * p, 2)]).then_inc(s_y_out, 16)

            with sp.Fori(0, LOOPS) as g:
                for slot in range(2):
                    sp.wait_ge(s_xt, 2 * (2 * g + slot) + 2)
                    load(2 * g + slot + 2, slot)
                    store(2 * g + slot)
            store(PAIRS - 2)
            sp.wait_ge(s_y_copied, 2 + TILES - 1)
            sp.dma_start(out_tile[TILES - 2], y_sb[:, TILES - 2]).then_inc(s_y_out, 16)
            sp.wait_ge(s_last, 2)
            sp.dma_start(out_tile[TILES - 1], y_sb[:, TILES - 1]).then_inc(s_y_out, 16)
            sp.wait_ge(s_y_out, 16 * (PAIRS + 1))

        @blk.gpsimd
        def _(pool):
            nc.gpsimd.iota(p_num[:], pattern=[[0, 1]], base=0, channel_multiplier=1,
                           allow_small_or_imprecise_dtypes=True).then_inc(s_pool, 1)
            pool.wait_ge(s_pool, 1)
            nc.gpsimd.memset(ident[:], 0.0).then_inc(s_pool, 1)
            pool.wait_ge(s_pool, 2)
            nc.gpsimd.affine_select(out=ident[:], in_=ident[:], compare_op=ALU.not_equal, fill=1.0, base=0,
                                    pattern=[[-1, P]], channel_multiplier=1).then_inc(s_pool, 1)
            pool.wait_ge(s_pool, 3)
            nc.gpsimd.memset(fold_id[:], 0.0).then_inc(s_pool, 1)
            for j in range(Q):
                pool.wait_ge(s_pool, 4 + j)
                nc.gpsimd.affine_select(out=fold_id[:], in_=fold_id[:], compare_op=ALU.not_equal, fill=1.0,
                                        base=-R * j, pattern=[[-1, R]], channel_multiplier=1).then_inc(s_pool, 1)

            def gather(t):
                nc.gpsimd.indirect_dma_start(
                    out=w0_sel[:, t, :], out_offset=None, in_=W0_rows,
                    in_offset=bass.IndirectOffsetOnAxis(ap=w0_row[:, t:t + 1], axis=0),
                ).then_inc(s_w0_in[t // 2 % 2], 16)

            pool.wait_ge(s_a_in, 16)
            nc.gpsimd.tensor_tensor(a_diff[:], a_sb[:, 1:NL].rearrange("p l c r -> p c l r"),
                                    a_sb[:, 0].unsqueeze(2).broadcast_to([P, C, Q, R]),
                                    ALU.subtract).then_inc(s_adiff, 1)
            pool.wait_ge(s_adiff, 1)
            pool.wait_ge(s_adhi, 1)
            nc.gpsimd.tensor_tensor(ad_lo[:], a_diff[:], ad_hi[:].bitcast(F32), ALU.subtract).then_inc(s_adlo, 1)
            pool.wait_ge(s_w0_row, BT)
            for p in range(PAIRS):
                if p >= 2:
                    pool.wait_ge(s_diag32, p - 1)
                gather(2 * p)
                gather(2 * p + 1)

        @blk.scalar
        def _(act):
            act.dma_start(w_sb[:, 0], W[0:P, :]).then_inc(s_w_in[0], 16)

            act.dma_start(a_sb[:].rearrange("p l c r -> p l (c r)"), A_cols).then_inc(s_a_in, 16)

            def split_x(t, slot, u):
                act.wait_ge(s_xt, t + 1)
                nc.scalar.activation(xt_hi[:, slot, :, P * u:P * (u + 1)], xt[:, u], COPY).then_inc(s_xhi, 1)

            def split_u(n, u, bank, cols=slice(0, O)):
                act.wait_ge(s_u, n + 1)
                nc.scalar.activation(u_hi[:, u, cols], p_u[bank][:, cols], COPY).then_inc(s_uhi, 1)

            def copy_y(t, u):
                act.wait_ge(s_y, t + 1)
                nc.scalar.activation(y_sb[:, bass.ds(t, 1)], p_y[u][:].unsqueeze(1), COPY).then_inc(s_y_copied, 1)

            act.wait_ge(s_bT, 1)
            nc.scalar.activation(b_hi[:], p_y[0][:], COPY).then_inc(s_stack_hi, 1)
            act.wait_ge(s_adiff, 1)
            nc.scalar.activation(ad_hi[:], a_diff[:], COPY).then_inc(s_adhi, 1)
            act.wait_ge(s_aT, 1)
            nc.scalar.activation(a0_hi[:], p_y[1][:], COPY).then_inc(s_stack_hi, 1)
            split_x(0, 0, 0)
            act.wait_ge(s_less_hi, 1)
            nc.scalar.activation(b_stack[:], p_fold[:], COPY).then_inc(s_y_copied, 1)
            split_x(1, 0, 1)
            act.wait_ge(s_less_hi, 2)
            nc.scalar.activation(a0_stack[:], p_low[:], COPY).then_inc(s_y_copied, 1)

            def split_m(c):
                act.wait_ge(s_m, c + 1)
                nc.scalar.activation(m_hi[:, c], p_u[c][:], COPY).then_inc(s_uhi, 1)

            for c in range(C):
                split_m(c)

            def pair(p, slot, first=False, last=False):
                act.wait_ge(s_kept, p + 1)
                nc.scalar.activation(kept_hi[:], kept[:], COPY).then_inc(s_kepthi, 1)
                for u in range(2):
                    if not first:
                        copy_y(2 * p - 2 + u, u)
                    if not last:
                        split_x(2 * p + 2 + u, 1 - slot, u)
                    if u == 0:
                        act.wait_ge(s_fold, p + 1)
                        nc.scalar.activation(low_stack[:], p_fold[:, 0:ROWS], COPY).then_inc(s_foldhi, 1)
                act.wait_ge(s_diag32, p + 1)
                nc.scalar.activation(diag_hi[:, slot], diag[:, slot], COPY).then_inc(s_diaghi, 1)
                if not last:
                    split_u(2 * p, 0, 2 * slot)
                    split_u(2 * p + 1, 1, 2 * slot + 1)

            pair(0, 0, first=True)
            with act.Fori(0, LOOPS) as g:
                for slot in (1, 0):
                    pair(2 * g + 2 - slot, slot)
            pair(PAIRS - 1, 1, last=True)
            split_u(TILES - 2, 1, 3, left)
            split_u(TILES - 1, 0, 2)
            split_u(TILES, 1, 0, right)
            copy_y(TILES - 2, 0)

        @blk.vector
        def _(dve):
            chain = [0]

            def then_wait(ins):
                chain[0] += 1
                ins.then_inc(s_dve, 1)
                dve.wait_ge(s_dve, chain[0])

            def transpose_x(slot, u):
                nc.vector.transpose(xt[:, u].rearrange("p c (b s) -> p c b s", s=S),
                                    x_sb[:, slot, u].rearrange("p b (i c) -> p c b i", c=C)).then_inc(s_xt, 1)

            def split_x(t, slot, u):
                dve.wait_ge(s_xhi, t + 1)
                cols = slice(P * u, P * (u + 1))
                nc.vector.tensor_tensor(xt_lo[:, slot, :, cols], xt[:, u], xt_hi[:, slot, :, cols].bitcast(F32),
                                        ALU.subtract).then_inc(s_xlo, 1)

            def split_u(n, u, bank, cols=slice(0, O)):
                dve.wait_ge(s_uhi, C + n + 1)
                nc.vector.tensor_tensor(u_lo[:, u, cols], p_u[bank][:, cols], u_hi[:, u, cols].bitcast(F32),
                                        ALU.subtract).then_inc(s_ulo, 1)

            def keep_low(p):
                dve.wait_ge(s_low, p + 1)
                labels = keep[:, bass.ds(2 * BT * p, 2 * BT)].unsqueeze(2).broadcast_to([P, 2 * BT, S])
                nc.vector.tensor_tensor(kept[:].rearrange("p (b s) -> p b s", s=S),
                                        p_low[:, 0:ROWS].rearrange("p (b s) -> p b s", s=S),
                                        labels, ALU.mult).then_inc(s_kept, 1)

            def split_low(p):
                dve.wait_ge(s_kepthi, p + 1)
                nc.vector.tensor_tensor(kept_lo[:], kept[:], kept_hi[:].bitcast(F32),
                                        ALU.subtract).then_inc(s_keptlo, 1)

            for j in range(BT):
                nc.vector.memset(group[R * j:R * (j + 1)], float(j)).then_inc(s_group, 1)
            nc.vector.memset(block[:], 0.0).then_inc(s_group, 1)
            dve.wait_ge(s_group, BT + 1)
            for j in range(BT):
                nc.vector.memset(block[R * j:R * (j + 1), j:j + 1], 1.0).then_inc(s_group, 1)
            dve.wait_ge(s_pool, 1)
            then_wait(nc.vector.scalar_tensor_tensor(row_of[:], group[:], -float(R), p_num[:], ALU.mult, ALU.add))
            dve.wait_ge(s_bw_in, 16)
            nc.vector.tensor_scalar(bw_rep[:], bw_sb[:].unsqueeze(2).broadcast_to([P, OC, Q, R]), 0.5, None,
                                    ALU.mult).then_inc(s_rep, 1)
            dve.wait_ge(s_cond_in, 16)
            cond_v = cond_b[:].rearrange("p (k b) -> p b k", b=BT)
            for j in range(BT):
                quad = slice(R * j, R * (j + 1))
                nc.vector.tensor_scalar(w0_row[quad], cond_v[quad, j], float(S), row_of[quad, 0:1],
                                        ALU.mult, ALU.add).then_inc(s_w0_row, 1)

            def add_identity(o):
                dve.wait_ge(s_w_in[o], 16)
                w_diag = w_sb[:, o, P * o:P * (o + 1)]
                nc.vector.tensor_tensor(w_diag, w_diag, ident[:], ALU.add).then_inc(s_diag, 1)

            dve.wait_ge(s_a_in, 16)
            nc.vector.tensor_copy(a0_rep[:], a_sb[:, 0].unsqueeze(2).broadcast_to([P, C, Q, R])).then_inc(s_rep, 1)
            for j in range(Q):
                quad = slice(R * j, R * (j + 1))
                nc.vector.memset(b_lo_groups[quad], -float(j % 2)).then_inc(s_negative, 1)
                nc.vector.memset(a_lo_groups[quad], -float(j // 2)).then_inc(s_negative, 1)
            dve.wait_ge(s_negative, 2 * Q)
            dve.wait_ge(s_pool, 3)
            for to, groups in ((b_negative, b_lo_groups), (a_negative, a_lo_groups)):
                nc.vector.tensor_scalar(to[:], ident[:], groups[:, 0:1], None, ALU.mult).then_inc(s_negative, 1)

            dve.wait_ge(s_pool, 4 + Q)
            add_identity(0)
            dve.wait_ge(s_x_in[0], 16 * Q)
            transpose_x(0, 0)
            transpose_x(0, 1)
            add_identity(1)
            add_identity(2)
            split_x(0, 0, 0)
            add_identity(3)
            split_x(1, 0, 1)
            nc.vector.tensor_copy(fold_r[:], fold_id[:].unsqueeze(1).broadcast_to([P, Q, R])).then_inc(s_group, 1)
            dve.wait_ge(s_label_in, 16)
            nc.vector.tensor_scalar(keep[:], label_b[:], -1.0, group[:, 0:1], ALU.add,
                                    ALU.is_equal).then_inc(s_group, 1)

            def split_m(c):
                dve.wait_ge(s_uhi, c + 1)
                nc.vector.tensor_tensor(m_lo[:, c], p_u[c][:], m_hi[:, c].bitcast(F32),
                                        ALU.subtract).then_inc(s_mlo, 1)

            dve.wait_ge(s_group, 2 * BT + 3)
            for c in range(C - 1):
                split_m(c)
            keep_low(0)
            split_m(C - 1)
            split_low(0)
            before_pairs = chain[0]

            def pair(p, slot, used, landed, first=False, last=False):
                if not first:
                    keep_low(p)
                if not last:
                    dve.wait_ge(s_x_in[1 - slot], 16 * Q * landed)
                    transpose_x(1 - slot, 0)
                if not first:
                    split_low(p)
                if not last:
                    transpose_x(1 - slot, 1)
                    split_x(2 * p + 2, 1 - slot, 0)
                dve.wait_ge(s_foldhi, p + 1)
                nc.vector.tensor_tensor(low_stack[P // 2:P], p_fold[P // 2:P, 0:ROWS],
                                        low_stack[P // 2:P].bitcast(F32), ALU.subtract).then_inc(s_stack, 1)
                dve.wait_ge(s_w0_in[slot], 32 * used)
                nc.vector.tensor_tensor(mix[:, slot], w0_sel[:, bass.ds(2 * p, 2)],
                                        fold_id[:].unsqueeze(1).broadcast_to([P, 2, S]), ALU.add).then_inc(s_dve, 1)
                dve.wait_ge(s_dve, before_pairs + p + 1)
                nc.vector.tensor_tensor(diag[:, slot], mix[:, slot].unsqueeze(2).broadcast_to([P, 2, BT, S]),
                                        block[:].unsqueeze(1).unsqueeze(3).broadcast_to([P, 2, BT, S]),
                                        ALU.mult).then_inc(s_diag32, 1)
                if not last:
                    split_x(2 * p + 3, 1 - slot, 1)
                dve.wait_ge(s_diaghi, p + 1)
                nc.vector.tensor_tensor(diag_lo[:, slot], diag[:, slot], diag_hi[:, slot].bitcast(F32),
                                        ALU.subtract).then_inc(s_diaglo, 1)
                if not last:
                    split_u(2 * p, 0, 2 * slot)
                    split_u(2 * p + 1, 1, 2 * slot + 1)

            pair(0, 0, used=1, landed=1, first=True)
            with dve.Fori(0, LOOPS) as g:
                for slot in (1, 0):
                    pair(2 * g + 2 - slot, slot, used=g + 2 - slot, landed=g + 2)
            pair(PAIRS - 1, 1, used=PAIRS // 2, landed=None, last=True)
            split_u(TILES - 2, 1, 3, left)
            split_u(TILES - 1, 0, 2)
            split_u(TILES, 1, 0, right)
            for i, (bank, cols) in enumerate(((p_y[1], left), (p_u[1], right))):
                dve.wait_ge(s_y, TILES + i)
                nc.vector.tensor_copy(y_sb[:, TILES - 1, cols], bank[:, cols]).then_inc(s_last, 1)

        @blk.tensor
        def _(pe):
            mm = nc.tensor.matmul

            def low_pair(slot):
                for c in range(C):
                    mm(p_low[:, 0:ROWS], ad_hi[:, c], xt_hi[:, slot, c], start=(c == 0), stop=False)
                    mm(p_low[:, 0:ROWS], ad_hi[:, c], xt_lo[:, slot, c], start=False, stop=False)
                    last = mm(p_low[:, 0:ROWS], ad_lo[:, c], xt_hi[:, slot, c], start=False, stop=(c == C - 1))
                last.then_inc(s_low, 1)

            def main_tile(bank, slot, u, cols=slice(0, O), waits=False):
                to = p_u[bank][:, cols]
                rows = slice(P * u, P * (u + 1))
                for c in range(C):
                    if waits:
                        pe.wait_ge(s_mlo, c + 1)
                    mm(to, xt_hi[:, slot, c, rows], m_hi[:, c, cols], start=(c == 0), stop=False)
                    mm(to, xt_hi[:, slot, c, rows], m_lo[:, c, cols], start=False, stop=False)
                    mm(to, xt_lo[:, slot, c, rows], m_hi[:, c, cols], start=False, stop=False)

            def fold_pair():
                mm(p_fold[:, 0:ROWS], fold_r[:], kept_hi[:], start=True, stop=False)
                mm(p_fold[:, 0:ROWS], fold_r[:], kept_lo[:], start=False, stop=True).then_inc(s_fold, 1)

            def delta_tile(bank, u, cols=slice(0, O)):
                mm(p_u[bank][:, cols], low_stack[:, P * u:P * (u + 1)], b_stack[:, cols],
                   start=False, stop=True).then_inc(s_u, 1)

            def mix_tile(n, slot, u, to, cols=slice(0, O)):
                pe.wait_ge(s_uhi, C + n + 1)
                mm(to[:, cols], diag_hi[:, slot, u], u_hi[:, u, cols], start=True, stop=False)
                mm(to[:, cols], diag_lo[:, slot, u], u_hi[:, u, cols], start=False, stop=False)
                pe.wait_ge(s_ulo, n + 1)
                mm(to[:, cols], diag_hi[:, slot, u], u_lo[:, u, cols], start=False, stop=True).then_inc(s_y, 1)

            def transpose_w(o):
                pe.wait_ge(s_diag, o + 1)
                rows_t = w_sb[:, o].rearrange("p (t c) -> p c t", c=C)
                for c in range(C):
                    mm(p_u[c][:, P * o:P * (o + 1)], rows_t[:, c], ident[:], start=(o == 0), stop=False,
                       is_transpose=True)

            pe.wait_ge(s_pool, 3)
            for i in range(WARM):
                mm(p_low[:, 0:P], ident[:], ident[:], start=True, stop=True)

            def transpose_groups(bank, source, close):
                for c in range(C):
                    last = mm(bank[:, P * c:P * (c + 1)], source[:, c], ident[:], start=(c == 0),
                              stop=(close and c == C - 1), is_transpose=True)
                return last

            pe.wait_ge(s_rep, 1)
            transpose_groups(p_y[0], bw_rep, True).then_inc(s_bT, 1)
            pe.wait_ge(s_rep, 2)
            transpose_groups(p_y[1], a0_rep, True).then_inc(s_aT, 1)
            transpose_groups(p_fold, bw_rep, False)
            transpose_groups(p_low, a0_rep, False)
            pe.wait_ge(s_negative, 2 * (Q + 1))
            pe.wait_ge(s_stack_hi, 1)
            mm(p_fold[:], b_negative[:], b_hi[:], start=False, stop=True).then_inc(s_less_hi, 1)
            pe.wait_ge(s_stack_hi, 2)
            mm(p_low[:], a_negative[:], a0_hi[:], start=False, stop=True).then_inc(s_less_hi, 1)
            for o in range(OC):
                transpose_w(o)
            pe.wait_ge(s_y_copied, 2)
            for c in range(C):
                mm(p_u[c][:], a0_stack[:, P * c:P * (c + 1)], b_stack[:], start=False, stop=True).then_inc(s_m, 1)
            pe.wait_ge(s_adlo, 1)

            def pair(p, slot, first=False, last=False):
                pe.wait_ge(s_xlo, 2 * p + 2)
                low_pair(slot)
                if not first:
                    pe.wait_ge(s_diaglo, p)
                    pe.wait_ge(s_y_copied, 2 * p - 1)
                    mix_tile(2 * p - 2, 1 - slot, 0, p_y[0])
                main_tile(2 * slot, slot, 0, waits=first)
                pe.wait_ge(s_keptlo, p + 1)
                fold_pair()
                if not first:
                    pe.wait_ge(s_y_copied, 2 * p)
                    mix_tile(2 * p - 1, 1 - slot, 1, p_y[1])
                if not last:
                    main_tile(2 * slot + 1, slot, 1)
                    pe.wait_ge(s_stack, p + 1)
                    delta_tile(2 * slot, 0)
                    delta_tile(2 * slot + 1, 1)

            pair(0, 0, first=True)
            with pe.Fori(0, LOOPS) as g:
                for slot in (1, 0):
                    pair(2 * g + 2 - slot, slot)
            pair(PAIRS - 1, 1, last=True)
            main_tile(3, 1, 1, left)
            pe.wait_ge(s_stack, PAIRS)
            delta_tile(3, 1, left)
            delta_tile(2, 0)
            main_tile(0, 1, 1, right)
            delta_tile(0, 1, right)
            pe.wait_ge(s_diaglo, PAIRS)
            pe.wait_ge(s_y_copied, TILES)
            mix_tile(TILES - 1, 1, 0, p_y[0])
            mix_tile(TILES - 2, 1, 1, p_y[1], left)
            mix_tile(TILES, 1, 1, p_u[1], right)


_INS = ["x", "itok_B_0_15", "itok_B_0_2", "L0_cond_weights", "L1_cond_W", "L1_cond_lora_A", "L1_cond_lora_B_w"]


def kernel(**inputs):
    import numpy as np
    import concourse.bacc as bacc
    from concourse.bass_utils import run_bass_kernel_spmd

    nc = bacc.Bacc("TRN2", target_bir_lowering=False, num_devices=1)
    arrays, args = {}, []
    for name in _INS:
        a = np.ascontiguousarray(inputs[name])
        arrays[f"in_{name}"] = a
        args.append(nc.dram_tensor(f"in_{name}", a.shape, mybir.dt.from_np(a.dtype), kind="ExternalInput").ap())
    shape = inputs["x"].shape
    out = nc.dram_tensor("out_0", shape, F32, kind="ExternalOutput").ap()
    conditioned_lora_kernel(nc, *args, out)
    r = run_bass_kernel_spmd(nc, [arrays], core_ids=[0])
    return r.results[0]["out_0"]
```
